# Optimizing a Trainium2 kernel written in Bass

```python
import numpy as np
import jax
import jax.numpy as jnp

def _softmax(x, axis=-1):
    return jax.nn.softmax(x, axis=axis)

def _gelu(x):
    return jax.nn.gelu(x, approximate=True)

def _silu(x):
    return jax.nn.silu(x)

def _sigmoid(x):
    return jax.nn.sigmoid(x)

def _layernorm(x, axis=-1, eps=1e-05):
    m = jnp.mean(x, axis=axis, keepdims=True)
    v = jnp.var(x, axis=axis, keepdims=True)
    return (x - m) / jnp.sqrt(v + eps)

def _scatter_add(tgt, idx, src, axis=0):
    return tgt.at[idx].add(src)

def _segment_sum(src, seg, n):
    return jax.ops.segment_sum(src, seg, n)
kernel_name = 'mk_conv_seq_d1_conv_nhwc512_r2_ec8667'

def setup_inputs(seed: int=0):
    np.random.seed(seed)
    _w = jnp.asarray

    def _rec_inputs():
        import jax
        import jax.numpy as jnp
        _gk = jax.random.key(seed)
        x = -0.000125 + 0.9999 * jax.random.normal(jax.random.fold_in(_gk, 1), (16, 32, 32, 256), jnp.float32)
        return x
    x = _rec_inputs()

    def _L0_conv_setup():
        import jax, jax.numpy as jnp
        import numpy as np
        C = 256

        def _maxpool2x2(x):
            B, H, W, Cc = x.shape
            return x.reshape(B, H // 2, 2, W // 2, 2, Cc).max(axis=(2, 4))
        key = jax.random.key(seed)
        ks = jax.random.split(key, 6)
        x = jax.random.normal(ks[0], (16, 32, 32, C), dtype=jnp.float32)
        s = lambda k, i, o: jax.random.normal(k, (i, o), dtype=jnp.float32) / np.sqrt(i)
        W_theta = s(ks[1], C, C // 8)
        W_phi = s(ks[2], C, C // 8)
        W_g = s(ks[3], C, C // 2)
        W_o = s(ks[4], C // 2, C)
        gamma = jnp.float32(0.7)
        return {'x': x, 'W_theta': W_theta, 'W_phi': W_phi, 'W_g': W_g, 'W_o': W_o, 'gamma': gamma}
    _L0_conv_all = _L0_conv_setup()
    _L0_conv_in = {k: v for k, v in _L0_conv_all.items() if k in ('W_theta', 'W_phi', 'W_g', 'W_o', 'gamma')}
    del _L0_conv_all
    return {'x': x, 'L0_conv_W_theta': _L0_conv_in['W_theta'], 'L0_conv_W_phi': _L0_conv_in['W_phi'], 'L0_conv_W_g': _L0_conv_in['W_g'], 'L0_conv_W_o': _L0_conv_in['W_o'], 'L0_conv_gamma': _L0_conv_in['gamma']}

def reference(x, L0_conv_W_theta, L0_conv_W_phi, L0_conv_W_g, L0_conv_W_o, L0_conv_gamma):
    import jax
    import jax.numpy as jnp

    def _L0_conv_ref(x, W_theta, W_phi, W_g, W_o, gamma):
        import jax, jax.numpy as jnp
        import numpy as np
        C = 256

        def _maxpool2x2(x):
            B, H, W, Cc = x.shape
            return x.reshape(B, H // 2, 2, W // 2, 2, Cc).max(axis=(2, 4))
        B, H, W, Cc = x.shape
        S = H * W
        Sk = S // 4
        theta = jnp.einsum('bhwc,cd->bhwd', x, W_theta)
        phi = _maxpool2x2(jnp.einsum('bhwc,cd->bhwd', x, W_phi))
        g = _maxpool2x2(jnp.einsum('bhwc,cd->bhwd', x, W_g))
        theta = theta.reshape(B, S, Cc // 8)
        phi = phi.reshape(B, Sk, Cc // 8)
        g = g.reshape(B, Sk, Cc // 2)
        beta = jax.nn.softmax(jnp.einsum('bqd,bkd->bqk', theta, phi), axis=-1)
        tmp = jnp.einsum('bqk,bkv->bqv', beta, g).reshape(B, H, W, Cc // 2)
        o = jnp.einsum('bhwv,vc->bhwc', tmp, W_o)
        return gamma * o + x

    def _gn(v, G=32, eps=1e-05):
        B_, H_, W_, C_ = v.shape
        g = v.reshape(B_, H_, W_, G, C_ // G)
        m = jnp.mean(g, axis=(1, 2, 4), keepdims=True)
        s = jnp.var(g, axis=(1, 2, 4), keepdims=True)
        return ((g - m) / jnp.sqrt(s + eps)).reshape(v.shape)

    def _ln_c(v, eps=1e-06):
        m = jnp.mean(v, axis=-1, keepdims=True)
        s = jnp.var(v, axis=-1, keepdims=True)
        return (v - m) / jnp.sqrt(s + eps)

    def _ln_t(v, eps=1e-05):
        m = jnp.mean(v, axis=-1, keepdims=True)
        s = jnp.var(v, axis=-1, keepdims=True)
        return (v - m) / jnp.sqrt(s + eps)

    def _to_tokens(v):
        B_, H_, W_, C_ = v.shape
        return v.reshape(B_, H_ * W_, C_)

    def _from_tokens(t, like):
        return t.reshape(like.shape)
    x = _L0_conv_ref(x, L0_conv_W_theta, L0_conv_W_phi, L0_conv_W_g, L0_conv_W_o, L0_conv_gamma)
    return x

_drawn_inputs = setup_inputs


def setup_inputs(seed=0):
    import zlib

    import numpy as np

    out = dict(_drawn_inputs(seed))
    spreads = {}
    factors = {}
    for name, (base, spread) in spreads.items():
        noise = np.random.default_rng([zlib.crc32(name.encode()), seed]).standard_normal(out[name].shape)
        drawn = base * np.exp(spread * noise) if base else spread * noise
        out[name] = jnp.asarray(drawn.astype(out[name].dtype))
    for name, factor in factors.items():
        out[name] = (out[name] * factor).astype(out[name].dtype)
    return out
```

```python
import concourse.bass as bass
from concourse import mybir
from contextlib import ExitStack

B, H, W, C = 16, 32, 32, 256
P = 128
DK = C // 8
DV = C // 2
Q = H * W
NK = Q // 4
WIN = 4
TILES = Q // P
CC = C // P
KC = NK // P
HALF = Q // 2
HT = TILES // 2
SLOTS = 3
TURNS = (B - 3) // SLOTS
THETA = 3 * DK
STACK = THETA + 2
GW = C + 2


class Image:

    def __init__(self, turn, k):
        self.turn, self.k = turn, k

    def at(self, more):
        return Image(self.turn, self.k + more)

    @property
    def number(self):
        return self.turn * SLOTS + self.k

    @property
    def slot(self):
        return self.k % SLOTS

    def is_number(self, n):
        return isinstance(self.turn, int) and self.number == n

    def count(self, per_image, n):
        return self.number * per_image + (n + 1)

    def dma_count(self):
        return (self.turn + (self.k // SLOTS + 1)) * 16


def nonlocal_block(nc, x, w_theta, w_phi, w_g, w_o, gamma, out):
    f32, f32r = mybir.dt.float32, mybir.dt.float32r
    ALU = mybir.AluOpType
    ACT = mybir.ActivationFunctionType
    AX = mybir.AxisListType

    def by_cell(t):
        return t.rearrange("b (j yp dy) (xp dx) c -> b j xp yp dy (dx c)", j=2, dy=2, dx=2)

    x_cells, out_cells = by_cell(x), by_cell(out)

    ctx = ExitStack()
    with ctx:
        def sb(name, shape, dt=f32):
            return ctx.enter_context(nc.sbuf_tensor(name, shape, dt))

        def bank(name):
            return ctx.enter_context(nc.psum_tensor(name, [P, HALF], f32))

        def sem(name):
            return ctx.enter_context(nc.semaphore(name))

        ident = sb("ident", [P, P])
        w_tp = sb("w_tp", [P, CC, P])
        w_tp_hi, w_tp_lo = sb("w_tp_hi", [P, CC, P], f32r), sb("w_tp_lo", [P, CC, P], f32r)
        w_g_sb = sb("w_g_sb", [P, CC, DV])
        w_g_hi, w_g_lo = sb("w_g_hi", [P, CC, DV], f32r), sb("w_g_lo", [P, CC, DV], f32r)
        w_o_sb, w_og = sb("w_o_sb", [P, C]), sb("w_og", [P, C])
        w_o_hi, w_o_lo = sb("w_o_hi", [P, C], f32r), sb("w_o_lo", [P, C], f32r)
        gamma_sb = sb("gamma_sb", [P, 1])
        x_sb = sb("x_sb", [P, SLOTS, TILES, C])
        y_sb = sb("y_sb", [P, TILES, C])
        xT_hi, xT_lo = sb("xT_hi", [P, CC, Q], f32r), sb("xT_lo", [P, CC, Q], f32r)
        theta = sb("theta", [P, SLOTS, Q], f32r)
        phi = sb("phi", [P, SLOTS, NK], f32r)
        phi_max = sb("phi_max", [P, NK])
        phi_hi = sb("phi_hi", [P, NK], f32r)
        g_max = sb("g_max", [P, NK])
        g_hi, g_lo = sb("g_hi", [P, NK], f32r), sb("g_lo", [P, NK], f32r)
        G_hi, G_lo = sb("G_hi", [P, KC, GW], f32r), sb("G_lo", [P, KC, GW], f32r)
        neg_max = sb("neg_max", [P, TILES])
        neg_parts = sb("neg_parts", [P, P])
        neg_rows = sb("neg_rows", [2 * TILES, P], f32r)
        e_sb = sb("e_sb", [P, KC, Q])
        e_hi, e_lo = sb("e_hi", [P, KC, Q], f32r), sb("e_lo", [P, KC, Q], f32r)
        r_sum = sb("r_sum", [P, TILES])

        turn_banks = [bank("turn0"), bank("turn1")]
        proj_banks = [bank("proj0"), bank("proj1")]
        score_banks = [bank("score0"), bank("score1")]
        out_banks = [bank("out0"), bank("out1")]
        G_bank, neg_bank = turn_banks[0], turn_banks[0]
        xT_bank = [turn_banks[1], turn_banks[1], turn_banks[0], turn_banks[1]]

        w_in = sem("w_in")
        const_ready = sem("const_ready")
        const_step = sem("const_step")
        ident_zero, ident_ready = sem("ident_zero"), sem("ident_ready")
        x_in = [[sem(f"x_in{s}{h}") for h in range(2)] for s in range(SLOTS)]
        y_out = [sem(f"y_out{h}") for h in range(2)]
        xT_turned = sem("xT_turned")
        xT_hi_ready, xT_lo_ready = sem("xT_hi_ready"), sem("xT_lo_ready")
        tp_ready, g_ready = sem("tp_ready"), sem("g_ready")
        theta_hi_ready, theta_lo_ready = sem("theta_hi_ready"), sem("theta_lo_ready")
        phi_pooled = sem("phi_pooled")
        phi_copied = sem("phi_copied")
        phi_lo_ready = sem("phi_lo_ready")
        g_pooled = sem("g_pooled")
        g_hi_ready, g_lo_ready = sem("g_hi_ready"), sem("g_lo_ready")
        G_ready = sem("G_ready")
        G_hi_ready, G_lo_ready = sem("G_hi_ready"), sem("G_lo_ready")
        score_ready = sem("score_ready")
        max_ready = sem("max_ready")
        neg_hi_ready, neg_lo_ready = sem("neg_hi_ready"), sem("neg_lo_ready")
        neg_turned = sem("neg_turned")
        neg_rows_ready = sem("neg_rows_ready")
        neg_in = [sem(f"neg_in{s}") for s in range(SLOTS)]
        shifted_ready = sem("shifted_ready")
        e_ready, e_lo_ready = sem("e_ready"), sem("e_lo_ready")
        out_ready = sem("out_ready")
        r_ready = sem("r_ready")
        y_ready = sem("y_ready")

        block = ctx.enter_context(nc.Block())

        def run(eng, step):
            step(Image(0, 0), front=True, back=False, turn=True)
            step(Image(0, 1), front=True, back=True, turn=True)
            with eng.Fori(0, TURNS) as turn:
                for k in range(2, 2 + SLOTS):
                    step(Image(turn, k), front=True, back=True, turn=True)
            for k in range(2 + TURNS * SLOTS, B):
                step(Image(0, k), front=True, back=True, turn=k + 1 < B)
            step(Image(0, B), front=False, back=True, turn=False)

        @block.sync
        def _(sp):
            def load(im, h):
                sp.dma_start(x_sb[:, im.slot, HT * h:HT * (h + 1), :].rearrange("p (dy dx) c -> p dy (dx c)", dy=2),
                             x_cells[im.number, h]).then_inc(x_in[im.slot][h], 16)

            def store(im, h):
                sp.wait_ge(y_ready, im.count(TILES, HT * h + HT - 1))
                sp.dma_start(out_cells[im.number, h],
                             y_sb[:, HT * h:HT * (h + 1), :].rearrange("p (dy dx) c -> p dy (dx c)", dy=2),
                             ).then_inc(y_out[h], 16)

            load(Image(0, 0), 0)
            load(Image(0, 0), 1)
            for n in range(3):
                sp.dma_start(w_tp[:, :, DK * n:DK * (n + 1)],
                             w_theta.rearrange("(a p) n -> p a n", p=P)).then_inc(w_in, 16)
            sp.dma_start(w_tp[:, :, THETA:P], w_phi.rearrange("(a p) n -> p a n", p=P)).then_inc(w_in, 16)
            sp.dma_start(w_g_sb[:, :, :], w_g.rearrange("(a p) n -> p a n", p=P)).then_inc(w_in, 16)
            sp.dma_start(w_o_sb[:, :], w_o).then_inc(w_in, 16)
            sp.dma_start(gamma_sb[:, :], gamma.partition_broadcast(P)).then_inc(w_in, 16)
            for n in range(1, SLOTS):
                load(Image(0, n), 0)
                load(Image(0, n), 1)

            def step(im, front, back, turn):
                if back:
                    for h in range(2):
                        store(im.at(-1), h)
                        if not any(im.at(SLOTS - 1).is_number(n) for n in (B, B + 1, B + 2)):
                            load(im.at(SLOTS - 1), h)

            run(sp, step)
            for h in range(2):
                sp.wait_ge(y_out[h], 16 * B)

        @block.tensor
        def _(pe):
            def turn_x(im, f):
                h, c = divmod(f, CC)
                pe.wait_ge(x_in[im.slot][h], im.dma_count())
                if f == 0:
                    if not im.is_number(0):
                        pe.wait_ge(xT_lo_ready, im.at(-1).count(4, 3))
                elif f == 2:
                    if not im.is_number(0):
                        pe.wait_ge(neg_rows_ready, im.at(-1).count(1, 0))
                else:
                    pe.wait_ge(xT_lo_ready, im.count(4, 0 if f == 1 else 1))
                for t in range(HT):
                    last = nc.tensor.transpose(xT_bank[f][:, P * t:P * (t + 1)],
                                               x_sb[:, im.slot, HT * h + t, P * c:P * (c + 1)], ident[:, :])
                last.then_inc(xT_turned, 1)

            def project(im, hi, lo, h, bank, done):
                n = 0
                for c in range(CC):
                    for w, xT in ((hi, xT_hi), (lo, xT_hi), (hi, xT_lo)):
                        last = nc.tensor.matmul(bank[:, :], w[:, c, :], xT[:, c, HALF * h:HALF * (h + 1)],
                                                start=(n == 0), stop=(n == 3 * CC - 1))
                        n += 1
                last.then_inc(done, 1)

            def theta_phi(im, h):
                pe.wait_ge(xT_lo_ready, im.count(4, CC * h + CC - 1))
                if not im.is_number(0):
                    pe.wait_ge(g_pooled, im.at(-1).count(2, h))
                project(im, w_tp_hi, w_tp_lo, h, proj_banks[h], tp_ready)

            def values(im, h):
                pe.wait_ge(theta_lo_ready, im.count(2, h))
                project(im, w_g_hi, w_g_lo, h, proj_banks[h], g_ready)

            def score(im, n):
                if n == 0:
                    pe.wait_ge(theta_lo_ready, im.count(2, 1))
                    pe.wait_ge(phi_lo_ready, im.count(1, 0))
                if n >= 2:
                    pe.wait_ge(max_ready, im.count(4, n - 2))
                elif not im.is_number(0):
                    pe.wait_ge(e_ready, im.at(-1).count(4, n + 2))
                for i in range(2):
                    t = 2 * n + i
                    last = nc.tensor.matmul(score_banks[n % 2][:, NK * i:NK * (i + 1)],
                                            theta[0:THETA, im.slot, P * t:P * (t + 1)],
                                            phi[0:THETA, im.slot, :], start=(i == 0), stop=True,
                                            skip_group_check=True)
                last.then_inc(score_ready, 1)

            def turn_max(im):
                pe.wait_ge(neg_lo_ready, im.count(1, 0))
                if not im.is_number(0):
                    pe.wait_ge(G_lo_ready, im.at(-1).count(1, 0))
                nc.tensor.transpose(neg_bank[:, 0:P], neg_parts[:, :], ident[:, :]).then_inc(neg_turned, 1)

            def shifted(im, n):
                h, k = divmod(n, KC)
                if n == 0:
                    pe.wait_ge(neg_in[im.slot], im.dma_count())
                if n < 2:
                    pe.wait_ge(max_ready, im.count(4, n + 2))
                else:
                    pe.wait_ge(e_ready, im.count(4, n - 2))
                nc.tensor.matmul(score_banks[n % 2][:, :], phi[0:STACK, im.slot, P * k:P * (k + 1)],
                                 theta[0:STACK, im.slot, HALF * h:HALF * (h + 1)],
                                 start=True, stop=True).then_inc(shifted_ready, 1)

            def mix(im):
                pe.wait_ge(g_hi_ready, im.count(1, 0))
                pe.wait_ge(g_lo_ready, im.count(1, 0))
                pe.wait_ge(xT_lo_ready, mix_frees(im))
                n = 0
                for k in range(KC):
                    cells = slice(P * k, P * (k + 1))
                    for g, w in ((g_hi, w_o_hi), (g_hi, w_o_lo), (g_lo, w_o_hi)):
                        last = nc.tensor.matmul(G_bank[:, C * k:C * (k + 1)], g[:, cells], w[:, :],
                                                start=(n == 0), stop=(n % 3 == 2), skip_group_check=True)
                        n += 1
                last.then_inc(G_ready, 1)

            def mix_frees(im):
                last = im.is_number(B - 1)
                return im.count(4, 3) if last else im.at(1).count(4, 2)

            def output(im, t):
                if t == 0:
                    pe.wait_ge(G_lo_ready, im.count(1, 0))
                if t % HT == 0:
                    pe.wait_ge(e_lo_ready, im.count(4, KC * (t // HT) + KC - 1))
                if not (im.is_number(0) and t < 2):
                    pe.wait_ge(y_ready, im.count(TILES, t - 2))
                n = 0
                for k in range(KC):
                    pixels = slice(P * t, P * (t + 1))
                    for e, G in ((e_hi, G_hi), (e_hi, G_lo), (e_lo, G_hi)):
                        last = nc.tensor.matmul(out_banks[t % 2][:, 0:GW], e[:, k, pixels], G[:, k, :],
                                                start=(n == 0), stop=(n == 3 * KC - 1))
                        n += 1
                last.then_inc(out_ready, 1)

            pe.wait_ge(ident_ready, 1)
            for f in range(4):
                turn_x(Image(0, 0), f)
            pe.wait_ge(const_ready, 1)

            def step(im, front, back, turn):
                old = im.at(-1)
                if back:
                    shifted(old, 0)
                if front:
                    theta_phi(im, 0)
                if back:
                    shifted(old, 1)
                if front:
                    theta_phi(im, 1)
                if back:
                    mix(old)
                    shifted(old, 2)
                if front:
                    values(im, 0)
                if back:
                    shifted(old, 3)
                if front:
                    values(im, 1)
                for t in range(TILES):
                    if front and t < 4:
                        score(im, t)
                    if turn and t == 4:
                        turn_x(im.at(1), 0)
                    if back:
                        output(old, t)
                    if front and t == 4:
                        turn_max(im)
                    if turn and t >= 4 and t < 7:
                        turn_x(im.at(1), t - 3)

            run(pe, step)

        @block.scalar
        def _(act):
            def x_hi(im, f):
                h, c = divmod(f, CC)
                act.wait_ge(xT_turned, im.count(4, f))
                if not im.is_number(0):
                    act.wait_ge(g_ready, im.at(-1).count(2, h))
                nc.scalar.copy(xT_hi[:, c, HALF * h:HALF * (h + 1)], xT_bank[f][:, :]).then_inc(xT_hi_ready, 1)

            def theta_hi(im, h):
                act.wait_ge(tp_ready, im.count(2, h))
                nc.scalar.copy(theta[0:THETA, im.slot, HALF * h:HALF * (h + 1)],
                               proj_banks[h][0:THETA, :]).then_inc(theta_hi_ready, 1)

            def phi_parts(im):
                act.wait_ge(phi_pooled, im.count(2, 1))
                if not im.is_number(0):
                    act.wait_ge(phi_lo_ready, im.at(-1).count(1, 0))
                pooled = phi_max[2 * DK:THETA, :]
                for dst in (phi_hi[2 * DK:THETA, :], phi[0:DK, im.slot, :], phi[DK:2 * DK, im.slot, :]):
                    nc.scalar.copy(dst, pooled).then_inc(phi_copied, 1)

            def exponentials(im, n):
                h, k = divmod(n, KC)
                pixels = slice(HALF * h, HALF * (h + 1))
                act.wait_ge(shifted_ready, im.count(4, n))
                if not im.is_number(0):
                    act.wait_ge(out_ready, im.at(-1).count(TILES, HT * h + HT - 1))
                    act.wait_ge(e_lo_ready, im.at(-1).count(4, n))
                nc.scalar.activation(e_hi[:, k, pixels], score_banks[n % 2][:, :], ACT.Exp)
                nc.scalar.activation(e_sb[:, k, pixels], score_banks[n % 2][:, :], ACT.Exp).then_inc(e_ready, 1)

            def G_high(im):
                act.wait_ge(G_ready, im.count(1, 0))
                if not im.is_number(0):
                    act.wait_ge(out_ready, im.at(-1).count(TILES, TILES - 1))
                nc.scalar.copy(G_hi[:, :, 0:C], G_bank[:, :].rearrange("p (k c) -> p k c", k=KC)).then_inc(G_hi_ready, 1)

            def g_high(im):
                act.wait_ge(g_pooled, im.count(2, 1))
                if not im.is_number(0):
                    act.wait_ge(G_ready, im.at(-1).count(1, 0))
                nc.scalar.copy(g_hi[:, :], g_max[:, :]).then_inc(g_hi_ready, 1)

            def max_rows(im):
                act.wait_ge(neg_turned, im.count(1, 0))
                if not im.is_number(0):
                    act.wait_ge(neg_in[(im.k - 1) % SLOTS], im.at(-1).dma_count())
                nc.scalar.copy(neg_rows[:, :], neg_bank[0:2 * TILES, 0:P]).then_inc(neg_rows_ready, 1)

            def max_into_stack(im):
                act.wait_ge(neg_rows_ready, im.count(1, 0))
                act.dma_start(theta[THETA:STACK, im.slot, :].bitcast(f32).rearrange("r (t n) -> r t n", t=TILES),
                              neg_rows[:, :].bitcast(f32)).then_inc(neg_in[im.slot], 16)

            for f in range(4):
                x_hi(Image(0, 0), f)

            def step(im, front, back, turn):
                old = im.at(-1)
                if back:
                    exponentials(old, 0)
                if front:
                    theta_hi(im, 0)
                if back:
                    exponentials(old, 1)
                if front:
                    theta_hi(im, 1)
                    phi_parts(im)
                if back:
                    G_high(old)
                    exponentials(old, 2)
                    exponentials(old, 3)
                if front:
                    g_high(im)
                if turn:
                    x_hi(im.at(1), 0)
                if front:
                    max_rows(im)
                if turn:
                    x_hi(im.at(1), 1)
                if front:
                    max_into_stack(im)
                if turn:
                    x_hi(im.at(1), 2)
                    x_hi(im.at(1), 3)

            run(act, step)

        @block.gpsimd
        def _(pool):
            nc.gpsimd.memset(ident[:, :], 0.0).then_inc(ident_zero, 1)
            pool.wait_ge(ident_zero, 1)
            nc.gpsimd.affine_select(out=ident[:, :], in_=ident[:, :], compare_op=ALU.not_equal, fill=1.0,
                                    base=0, pattern=[[-1, P]], channel_multiplier=1).then_inc(ident_ready, 1)

            def e_low(im, n):
                h, k = divmod(n, KC)
                pixels = slice(HALF * h, HALF * (h + 1))
                pool.wait_ge(e_ready, im.count(4, n))
                if not im.is_number(0):
                    pool.wait_ge(out_ready, im.at(-1).count(TILES, HT * h + HT - 1))
                nc.gpsimd.tensor_tensor(e_lo[:, k, pixels], e_sb[:, k, pixels], e_hi[:, k, pixels].bitcast(f32),
                                        ALU.subtract).then_inc(e_lo_ready, 1)

            def g_low(im):
                pool.wait_ge(g_hi_ready, im.count(1, 0))
                if not im.is_number(0):
                    pool.wait_ge(G_ready, im.at(-1).count(1, 0))
                nc.gpsimd.tensor_tensor(g_lo[:, :], g_max[:, :], g_hi[:, :].bitcast(f32),
                                        ALU.subtract).then_inc(g_lo_ready, 1)

            def step(im, front, back, turn):
                if back:
                    for n in range(4):
                        e_low(im.at(-1), n)
                if front:
                    g_low(im)

            run(pool, step)

        @block.vector
        def _(dve):
            v = nc.vector

            def x_lo(im, f):
                h, c = divmod(f, CC)
                pixels = slice(HALF * h, HALF * (h + 1))
                dve.wait_ge(xT_hi_ready, im.count(4, f))
                v.tensor_tensor(xT_lo[:, c, pixels], xT_bank[f][:, :], xT_hi[:, c, pixels].bitcast(f32),
                                ALU.subtract).then_inc(xT_lo_ready, 1)

            def phi_pool(im, h):
                dve.wait_ge(tp_ready, im.count(2, h))
                if h == 0 and not im.is_number(0):
                    dve.wait_ge(phi_lo_ready, im.at(-1).count(1, 0))
                v.tensor_reduce(phi_max[2 * DK:THETA, P * h:P * (h + 1)],
                                proj_banks[h][THETA:P, :].rearrange("p (w n) -> p n w", w=WIN),
                                AX.X, ALU.max).then_inc(phi_pooled, 1)

            def theta_lo(im, h):
                rows, pixels = slice(DK, 2 * DK), slice(HALF * h, HALF * (h + 1))
                dve.wait_ge(theta_hi_ready, im.count(2, h))
                v.tensor_tensor(theta[rows, im.slot, pixels], proj_banks[h][rows, :],
                                theta[rows, im.slot, pixels].bitcast(f32), ALU.subtract).then_inc(theta_lo_ready, 1)

            def phi_lo(im):
                rows = slice(2 * DK, THETA)
                dve.wait_ge(phi_copied, im.count(3, 2))
                v.tensor_tensor(phi[rows, im.slot, :], phi_max[rows, :], phi_hi[rows, :].bitcast(f32),
                                ALU.subtract).then_inc(phi_lo_ready, 1)

            def G_low(im):
                dve.wait_ge(G_hi_ready, im.count(1, 0))
                v.tensor_tensor(G_lo[:, :, 0:C], G_bank[:, :].rearrange("p (k c) -> p k c", k=KC),
                                G_hi[:, :, 0:C].bitcast(f32), ALU.subtract).then_inc(G_lo_ready, 1)

            def g_pool(im, h):
                dve.wait_ge(g_ready, im.count(2, h))
                if h == 0 and not im.is_number(0):
                    dve.wait_ge(g_lo_ready, im.at(-1).count(1, 0))
                v.tensor_reduce(g_max[:, P * h:P * (h + 1)], proj_banks[h][:, :].rearrange("p (w n) -> p n w", w=WIN),
                                AX.X, ALU.max).then_inc(g_pooled, 1)

            def maxima(im, n):
                dve.wait_ge(score_ready, im.count(4, n))
                v.tensor_reduce(neg_max[:, 2 * n:2 * n + 2],
                                score_banks[n % 2][:, :].rearrange("p (t k) -> p t k", t=2),
                                AX.X, ALU.max, negate=True).then_inc(max_ready, 1)

            def max_parts(im):
                dve.wait_ge(max_ready, im.count(4, 3))
                if not im.is_number(0):
                    dve.wait_ge(neg_turned, im.at(-1).count(1, 0))
                v.tensor_copy(neg_parts[:, 0:TILES].bitcast(f32r), neg_max[:, :]).then_inc(neg_hi_ready, 1)
                dve.wait_ge(neg_hi_ready, im.count(1, 0))
                v.tensor_tensor(neg_parts[:, TILES:2 * TILES], neg_max[:, :], neg_parts[:, 0:TILES],
                                ALU.subtract).then_inc(neg_lo_ready, 1)

            def reciprocal(im, t):
                dve.wait_ge(out_ready, im.count(TILES, t))
                v.reciprocal(r_sum[:, t:t + 1], out_banks[t % 2][:, C:C + 1]).then_inc(r_ready, 1)

            def finish(im, t):
                dve.wait_ge(r_ready, im.count(TILES, t))
                if t % HT == 0 and not im.is_number(0):
                    dve.wait_ge(y_out[t // HT], im.number * 16)
                v.scalar_tensor_tensor(y_sb[:, t, :], out_banks[t % 2][:, 0:C], r_sum[:, t:t + 1],
                                       x_sb[:, im.slot, t, :], ALU.mult, ALU.add).then_inc(y_ready, 1)

            v.memset(neg_parts[:, :], 0.0).then_inc(const_step, 1)
            v.memset(phi[THETA:STACK, :, :].bitcast(f32), 1.0).then_inc(const_step, 1)
            v.memset(G_hi[:, :, C:GW].bitcast(f32), 1.0).then_inc(const_step, 1)
            v.memset(G_lo[:, :, C:GW].bitcast(f32), 0.0).then_inc(const_step, 1)
            dve.wait_ge(w_in, 7 * 16)
            v.tensor_copy(w_tp_hi[:, :, :], w_tp[:, :, :]).then_inc(const_step, 1)
            v.tensor_copy(w_g_hi[:, :, :], w_g_sb[:, :, :]).then_inc(const_step, 1)
            v.tensor_scalar(w_og[:, :], w_o_sb[:, :], gamma_sb[:, 0:1], None, ALU.mult).then_inc(const_step, 1)
            dve.wait_ge(const_step, 7)
            v.tensor_copy(w_o_hi[:, :], w_og[:, :]).then_inc(const_step, 1)
            v.tensor_tensor(w_tp_lo[:, :, :], w_tp[:, :, :], w_tp_hi[:, :, :].bitcast(f32), ALU.subtract)
            v.tensor_tensor(w_g_lo[:, :, :], w_g_sb[:, :, :], w_g_hi[:, :, :].bitcast(f32), ALU.subtract)
            dve.wait_ge(const_step, 8)
            v.tensor_tensor(w_o_lo[:, :], w_og[:, :], w_o_hi[:, :].bitcast(f32), ALU.subtract).then_inc(const_ready, 1)

            for f in range(4):
                x_lo(Image(0, 0), f)

            def step(im, front, back, turn):
                old = im.at(-1)
                if front:
                    for h in range(2):
                        phi_pool(im, h)
                        theta_lo(im, h)
                    phi_lo(im)
                if back:
                    G_low(old)
                if front:
                    g_pool(im, 0)
                    g_pool(im, 1)
                for t in range(TILES + 1):
                    if front and t < 4:
                        maxima(im, t)
                    if front and t == 4:
                        max_parts(im)
                    if turn and 5 <= t:
                        x_lo(im.at(1), t - 5)
                    if back and t > 0:
                        finish(old, t - 1)
                    if back and t < TILES:
                        reciprocal(old, t)

            run(dve, step)


_INS = ["x", "L0_conv_W_theta", "L0_conv_W_phi", "L0_conv_W_g", "L0_conv_W_o", "L0_conv_gamma"]


def kernel(**inputs):
    import numpy as _np
    import concourse.bacc as _bacc
    from concourse import mybir as _mybir
    from concourse.bass_utils import run_bass_kernel_spmd as _run

    nc = _bacc.Bacc("TRN2", target_bir_lowering=False, num_devices=1)
    arrays, args = {}, []
    for name in _INS:
        a = _np.atleast_1d(_np.ascontiguousarray(inputs[name]))
        arrays[f"in_{name}"] = a
        args.append(nc.dram_tensor(f"in_{name}", a.shape, _mybir.dt.from_np(a.dtype), kind="ExternalInput").ap())
    out = nc.dram_tensor("out", (B, H, W, C), _mybir.dt.float32, kind="ExternalOutput").ap()
    nonlocal_block(nc, *args, out)
    r = _run(nc, [arrays], core_ids=[0])
    return r.results[0]["out"]
```

```python
import concourse.bass as bass
from concourse import mybir
from contextlib import ExitStack

B, H, W, C = 16, 32, 32, 256
P = 128
DK = C // 8
DV = C // 2
Q = H * W
NK = Q // 4
WIN = 4
TILES = Q // P
CC = C // P
KC = NK // P
HALF = Q // 2
HT = TILES // 2
SLOTS = 3
TURNS = (B - 3) // SLOTS
THETA = 3 * DK
STACK = THETA + 2
GW = C + 2


class Image:

    def __init__(self, turn, k):
        self.turn, self.k = turn, k

    def at(self, more):
        return Image(self.turn, self.k + more)

    @property
    def number(self):
        return self.turn * SLOTS + self.k

    @property
    def slot(self):
        return self.k % SLOTS

    def is_number(self, n):
        return isinstance(self.turn, int) and self.number == n

    def count(self, per_image, n):
        return self.number * per_image + (n + 1)

    def dma_count(self):
        return (self.turn + (self.k // SLOTS + 1)) * 16


def nonlocal_block(nc, x, w_theta, w_phi, w_g, w_o, gamma, out):
    f32, f32r = mybir.dt.float32, mybir.dt.float32r
    ALU = mybir.AluOpType
    ACT = mybir.ActivationFunctionType
    AX = mybir.AxisListType

    def by_cell(t):
        return t.rearrange("b (j yp dy) (xp dx) c -> b j xp yp dy (dx c)", j=2, dy=2, dx=2)

    x_cells, out_cells = by_cell(x), by_cell(out)

    ctx = ExitStack()
    with ctx:
        def sb(name, shape, dt=f32):
            return ctx.enter_context(nc.sbuf_tensor(name, shape, dt))

        def bank(name):
            return ctx.enter_context(nc.psum_tensor(name, [P, HALF], f32))

        def sem(name):
            return ctx.enter_context(nc.semaphore(name))

        ident = sb("ident", [P, P])
        w_t_sb, w_p_sb = sb("w_t_sb", [P, CC, DK]), sb("w_p_sb", [P, CC, DK])
        w_tp_hi, w_tp_lo = sb("w_tp_hi", [P, CC, P], f32r), sb("w_tp_lo", [P, CC, P], f32r)
        w_g_sb = sb("w_g_sb", [P, CC, DV])
        w_g_hi, w_g_lo = sb("w_g_hi", [P, CC, DV], f32r), sb("w_g_lo", [P, CC, DV], f32r)
        w_o_sb, w_og = sb("w_o_sb", [P, C]), sb("w_og", [P, C])
        w_o_hi, w_o_lo = sb("w_o_hi", [P, C], f32r), sb("w_o_lo", [P, C], f32r)
        gamma_sb = sb("gamma_sb", [P, 1])
        x_sb = sb("x_sb", [P, SLOTS, TILES, C])
        y_sb = sb("y_sb", [P, TILES, C])
        xT = sb("xT", [P, CC, Q])
        xT_hi, xT_lo = sb("xT_hi", [P, CC, Q], f32r), sb("xT_lo", [P, CC, Q], f32r)
        theta = sb("theta", [P, SLOTS, Q], f32r)
        phi = sb("phi", [P, SLOTS, NK], f32r)
        phi_max = sb("phi_max", [P, NK])
        phi_hi = sb("phi_hi", [P, NK], f32r)
        g_max = sb("g_max", [P, NK])
        g_hi, g_lo = sb("g_hi", [P, NK], f32r), sb("g_lo", [P, NK], f32r)
        G_sb = sb("G_sb", [P, KC * C])
        G_hi, G_lo = sb("G_hi", [P, SLOTS, KC, GW], f32r), sb("G_lo", [P, SLOTS, KC, GW], f32r)
        neg_max = sb("neg_max", [P, TILES])
        neg_parts = sb("neg_parts", [P, P])
        neg_rows = sb("neg_rows", [2 * TILES, P], f32r)
        e_sb = sb("e_sb", [P, KC, Q])
        e_hi, e_lo = sb("e_hi", [P, KC, Q], f32r), sb("e_lo", [P, KC, Q], f32r)
        r_sum = sb("r_sum", [P, TILES])

        turn_banks = [bank("turn0"), bank("turn1")]
        proj_banks = [bank("proj0"), bank("proj1")]
        score_banks = [bank("score0"), bank("score1")]
        out_banks = [bank("out0"), bank("out1")]
        neg_bank, G_bank = score_banks

        w_tp_in, w_g_in, w_o_in = sem("w_tp_in"), sem("w_g_in"), sem("w_o_in")
        w_hi_ready, w_lo_ready = sem("w_hi_ready"), sem("w_lo_ready")
        fixed_ready = sem("fixed_ready")
        w_og_ready = sem("w_og_ready")
        ident_zero, ident_ready = sem("ident_zero"), sem("ident_ready")
        x_in = [[sem(f"x_in{s}{h}") for h in range(2)] for s in range(SLOTS)]
        y_out = [sem(f"y_out{h}") for h in range(2)]
        last_out = [sem(f"last_out{dy}") for dy in range(2)]
        xT_turned = sem("xT_turned")
        xT_copied, xT_lo_ready = sem("xT_copied"), sem("xT_lo_ready")
        tp_ready, g_ready = sem("tp_ready"), sem("g_ready")
        theta_hi_ready, theta_lo_ready = sem("theta_hi_ready"), sem("theta_lo_ready")
        phi_pooled = sem("phi_pooled")
        phi_copied = sem("phi_copied")
        phi_lo_ready = sem("phi_lo_ready")
        g_pooled = sem("g_pooled")
        g_hi_ready, g_lo_ready = sem("g_hi_ready"), sem("g_lo_ready")
        G_ready = sem("G_ready")
        G_copied, G_lo_ready = sem("G_copied"), sem("G_lo_ready")
        score_ready = sem("score_ready")
        max_ready = sem("max_ready")
        neg_hi_ready, neg_lo_ready = sem("neg_hi_ready"), sem("neg_lo_ready")
        neg_turned = sem("neg_turned")
        neg_rows_ready = sem("neg_rows_ready")
        neg_in = [sem(f"neg_in{s}") for s in range(SLOTS)]
        shifted_ready = sem("shifted_ready")
        e_ready, e_lo_ready = sem("e_ready"), sem("e_lo_ready")
        e_lo_last = sem("e_lo_last")
        out_ready = sem("out_ready")
        r_ready = sem("r_ready")
        y_ready = sem("y_ready")

        block = ctx.enter_context(nc.Block())

        def on_vector(im):
            return im.is_number(0)

        def low_on_vector(im, n):
            return im.is_number(B - 1) and n % 2 == 1

        def run(eng, step):
            step(Image(0, 0), front=True, back=False, turn=True)
            step(Image(0, 1), front=True, back=True, turn=True)
            with eng.Fori(0, TURNS) as turn:
                for k in range(2, 2 + SLOTS):
                    step(Image(turn, k), front=True, back=True, turn=True)
            for k in range(2 + TURNS * SLOTS, B):
                step(Image(0, k), front=True, back=True, turn=k + 1 < B)
            step(Image(0, B), front=False, back=True, turn=False)

        @block.sync
        def _(sp):
            def load(im, h):
                sp.dma_start(x_sb[:, im.slot, HT * h:HT * (h + 1), :].rearrange("p (dy dx) c -> p dy (dx c)", dy=2),
                             x_cells[im.number, h]).then_inc(x_in[im.slot][h], 16)

            def store(im, h):
                sp.wait_ge(y_ready, im.count(TILES, HT * h + HT - 1))
                sp.dma_start(out_cells[im.number, h],
                             y_sb[:, HT * h:HT * (h + 1), :].rearrange("p (dy dx) c -> p dy (dx c)", dy=2),
                             ).then_inc(y_out[h], 16)

            def store_row(im, h, dy):
                t = HT * h + 2 * dy
                sp.wait_ge(y_ready, im.count(TILES, t + 1))
                sp.dma_start(out_cells[im.number, h, :, :, dy],
                             y_sb[:, t:t + 2, :].rearrange("p dx c -> p (dx c)")).then_inc(last_out[dy], 16)

            load(Image(0, 0), 0)
            sp.dma_start(w_t_sb[:, :, :], w_theta.rearrange("(a p) n -> p a n", p=P)).then_inc(w_tp_in, 16)
            sp.dma_start(w_p_sb[:, :, :], w_phi.rearrange("(a p) n -> p a n", p=P)).then_inc(w_tp_in, 16)
            sp.dma_start(w_g_sb[:, :, :], w_g.rearrange("(a p) n -> p a n", p=P)).then_inc(w_g_in, 16)
            load(Image(0, 0), 1)
            sp.dma_start(w_o_sb[:, :], w_o).then_inc(w_o_in, 16)
            sp.dma_start(gamma_sb[:, :], gamma.partition_broadcast(P)).then_inc(w_o_in, 16)
            for n in range(1, SLOTS):
                load(Image(0, n), 0)
                load(Image(0, n), 1)

            def max_into_stack(im):
                sp.wait_ge(neg_rows_ready, im.count(1, 0))
                sp.dma_start(theta[THETA:STACK, im.slot, :].bitcast(f32).rearrange("r (t n) -> r t n", t=TILES),
                             neg_rows[:, :].bitcast(f32)).then_inc(neg_in[im.slot], 16)

            def step(im, front, back, turn):
                if front:
                    max_into_stack(im)
                if back:
                    for h in range(2):
                        if im.is_number(B) and h == 1:
                            store_row(im.at(-1), h, 0)
                            store_row(im.at(-1), h, 1)
                        else:
                            store(im.at(-1), h)
                        if not any(im.at(SLOTS - 1).is_number(n) for n in (B, B + 1, B + 2)):
                            load(im.at(SLOTS - 1), h)

            run(sp, step)
            sp.wait_ge(y_out[0], 16 * B)
            sp.wait_ge(y_out[1], 16 * (B - 1))
            for dy in range(2):
                sp.wait_ge(last_out[dy], 16)

        @block.tensor
        def _(pe):
            def turn_x(im, f):
                h, c = divmod(f, CC)
                pe.wait_ge(x_in[im.slot][h], im.dma_count())
                user = im if f >= 2 else im.at(-1)
                if f >= 2 or not im.is_number(0):
                    pe.wait_ge(xT_lo_ready if on_vector(user) else xT_copied, user.count(4, (f - 2) % 4))
                for t in range(HT):
                    last = nc.tensor.transpose(turn_banks[f % 2][:, P * t:P * (t + 1)],
                                               x_sb[:, im.slot, HT * h + t, P * c:P * (c + 1)], ident[:, :])
                last.then_inc(xT_turned, 1)

            def project(im, hi, lo, h, bank, done):
                n = 0
                for c in range(CC):
                    for w, xT in ((hi, xT_hi), (lo, xT_hi), (hi, xT_lo)):
                        last = nc.tensor.matmul(bank[:, :], w[:, c, :], xT[:, c, HALF * h:HALF * (h + 1)],
                                                start=(n == 0), stop=(n == 3 * CC - 1))
                        n += 1
                last.then_inc(done, 1)

            def theta_phi(im, h):
                if im.is_number(0):
                    pe.wait_ge(w_lo_ready, 2)
                    pe.wait_ge(fixed_ready, 4)
                pe.wait_ge(xT_lo_ready, im.count(4, CC * h + CC - 1))
                if not im.is_number(0):
                    pe.wait_ge(g_pooled, im.at(-1).count(2, h))
                project(im, w_tp_hi, w_tp_lo, h, proj_banks[h], tp_ready)

            def values(im, h):
                if im.is_number(0):
                    pe.wait_ge(w_lo_ready, 3)
                pe.wait_ge(theta_lo_ready, im.count(2, h))
                project(im, w_g_hi, w_g_lo, h, proj_banks[h], g_ready)

            def score(im, n):
                if n == 0:
                    pe.wait_ge(theta_lo_ready, im.count(2, 1))
                    pe.wait_ge(phi_lo_ready, im.count(1, 0))
                if n >= 2:
                    pe.wait_ge(max_ready, im.count(4, n - 2))
                elif not im.is_number(0):
                    pe.wait_ge(e_ready, im.at(-1).count(4, n + 2))
                for i in range(2):
                    t = 2 * n + i
                    last = nc.tensor.matmul(score_banks[n % 2][:, NK * i:NK * (i + 1)],
                                            theta[0:THETA, im.slot, P * t:P * (t + 1)],
                                            phi[0:THETA, im.slot, :], start=(i == 0), stop=True,
                                            skip_group_check=True)
                last.then_inc(score_ready, 1)

            def turn_max(im):
                pe.wait_ge(neg_lo_ready, im.count(1, 0))
                pe.wait_ge(max_ready, im.count(4, 2))
                nc.tensor.transpose(neg_bank[:, 0:P], neg_parts[:, :], ident[:, :]).then_inc(neg_turned, 1)

            def shifted(im, n):
                h, k = divmod(n, KC)
                if n == 0:
                    pe.wait_ge(neg_rows_ready, im.count(1, 0))
                    pe.wait_ge(neg_in[im.slot], im.dma_count())
                elif n == 1:
                    pe.wait_ge(G_copied, im.count(1, 0))
                else:
                    pe.wait_ge(e_ready, im.count(4, n - 2))
                nc.tensor.matmul(score_banks[n % 2][:, :], phi[0:STACK, im.slot, P * k:P * (k + 1)],
                                 theta[0:STACK, im.slot, HALF * h:HALF * (h + 1)],
                                 start=True, stop=True).then_inc(shifted_ready, 1)

            def mix(im):
                if im.is_number(0):
                    pe.wait_ge(w_lo_ready, 4)
                pe.wait_ge(g_hi_ready, im.count(1, 0))
                pe.wait_ge(g_lo_ready, im.count(1, 0))
                pe.wait_ge(max_ready, im.count(4, 3))
                n = 0
                for k in range(KC):
                    cells = slice(P * k, P * (k + 1))
                    for g, w in ((g_hi, w_o_hi), (g_hi, w_o_lo), (g_lo, w_o_hi)):
                        last = nc.tensor.matmul(G_bank[:, C * k:C * (k + 1)], g[:, cells], w[:, :],
                                                start=(n == 0), stop=(n % 3 == 2), skip_group_check=True)
                        n += 1
                last.then_inc(G_ready, 1)

            def output(im, t):
                if t == 0:
                    pe.wait_ge(G_lo_ready, im.count(1, 0))
                if t % HT == 0:
                    if im.is_number(B - 1):
                        pe.wait_ge(e_lo_ready, im.count(4, t // HT))
                        pe.wait_ge(e_lo_last, t // HT + 1)
                    else:
                        pe.wait_ge(e_lo_ready, im.count(4, KC * (t // HT) + KC - 1))
                if not (im.is_number(0) and t < 2):
                    pe.wait_ge(y_ready, im.count(TILES, t - 2))
                n = 0
                for k in range(KC):
                    pixels = slice(P * t, P * (t + 1))
                    for e, G in ((e_hi, G_hi), (e_hi, G_lo), (e_lo, G_hi)):
                        last = nc.tensor.matmul(out_banks[t % 2][:, 0:GW], e[:, k, pixels], G[:, im.slot, k, :],
                                                start=(n == 0), stop=(n == 3 * KC - 1))
                        n += 1
                last.then_inc(out_ready, 1)

            pe.wait_ge(ident_ready, 1)
            for f in range(4):
                turn_x(Image(0, 0), f)

            def step(im, front, back, turn):
                old = im.at(-1)
                if front:
                    theta_phi(im, 0)
                if back:
                    shifted(old, 0)
                    shifted(old, 1)
                if front:
                    theta_phi(im, 1)
                if back:
                    shifted(old, 2)
                if front:
                    values(im, 0)
                if back:
                    shifted(old, 3)
                if front:
                    values(im, 1)
                for t in range(TILES):
                    if front and t < 4:
                        score(im, t)
                    if front and t == 5:
                        turn_max(im)
                    if front and t == 6:
                        mix(im)
                    if back:
                        output(old, t)
                    if turn and t < 4:
                        turn_x(im.at(1), t)

            run(pe, step)

        @block.scalar
        def _(act):
            def x_copies(im, f):
                h, c = divmod(f, CC)
                act.wait_ge(xT_turned, im.count(4, f))
                if not im.is_number(0):
                    act.wait_ge(g_ready, im.at(-1).count(2, h))
                    act.wait_ge(xT_lo_ready, im.at(-1).count(4, f))
                high = nc.scalar.copy(xT_hi[:, c, HALF * h:HALF * (h + 1)], turn_banks[f % 2][:, :])
                if on_vector(im):
                    high.then_inc(xT_copied, 1)
                    return
                nc.scalar.copy(xT[:, c, HALF * h:HALF * (h + 1)], turn_banks[f % 2][:, :]).then_inc(xT_copied, 1)

            def theta_hi(im, h):
                act.wait_ge(tp_ready, im.count(2, h))
                nc.scalar.copy(theta[0:THETA, im.slot, HALF * h:HALF * (h + 1)],
                               proj_banks[h][0:THETA, :]).then_inc(theta_hi_ready, 1)

            def exp_high(im, n):
                h, k = divmod(n, KC)
                pixels = slice(HALF * h, HALF * (h + 1))
                act.wait_ge(shifted_ready, im.count(4, n))
                if not im.is_number(0):
                    act.wait_ge(out_ready, im.at(-1).count(TILES, HT * h + HT - 1))
                nc.scalar.activation(e_hi[:, k, pixels], score_banks[n % 2][:, :], ACT.Exp)

            def exp_whole(im, n):
                h, k = divmod(n, KC)
                pixels = slice(HALF * h, HALF * (h + 1))
                if not im.is_number(0):
                    act.wait_ge(e_lo_ready, im.at(-1).count(4, n))
                nc.scalar.activation(e_sb[:, k, pixels], score_banks[n % 2][:, :], ACT.Exp).then_inc(e_ready, 1)

            def G_copies(im):
                act.wait_ge(G_ready, im.count(1, 0))
                if not im.is_number(0):
                    act.wait_ge(G_lo_ready, im.at(-1).count(1, 0))
                nc.scalar.copy(G_hi[:, im.slot, :, 0:C], G_bank[:, :].rearrange("p (k c) -> p k c", k=KC))
                nc.scalar.copy(G_sb[:, :], G_bank[:, :]).then_inc(G_copied, 1)

            def g_high(im):
                act.wait_ge(g_pooled, im.count(2, 1))
                if not im.is_number(0):
                    act.wait_ge(G_ready, im.at(-1).count(1, 0))
                nc.scalar.copy(g_hi[:, :], g_max[:, :]).then_inc(g_hi_ready, 1)

            def max_rows(im):
                act.wait_ge(neg_turned, im.count(1, 0))
                if not im.is_number(0):
                    act.wait_ge(neg_in[(im.k - 1) % SLOTS], im.at(-1).dma_count())
                nc.scalar.copy(neg_rows[:, :], neg_bank[0:2 * TILES, 0:P]).then_inc(neg_rows_ready, 1)


            for f in range(4):
                x_copies(Image(0, 0), f)

            def step(im, front, back, turn):
                old = im.at(-1)
                if front:
                    theta_hi(im, 0)
                if back:
                    exp_high(old, 0)
                    exp_whole(old, 0)
                    exp_high(old, 1)
                if front:
                    theta_hi(im, 1)
                if back:
                    exp_whole(old, 1)
                    for n in range(2, 4):
                        exp_high(old, n)
                        exp_whole(old, n)
                if front:
                    g_high(im)
                if turn:
                    for f in range(4):
                        x_copies(im.at(1), f)
                if front:
                    max_rows(im)
                    G_copies(im)

            run(act, step)

        @block.gpsimd
        def _(pool):
            nc.gpsimd.memset(ident[:, :], 0.0).then_inc(ident_zero, 1)
            pool.wait_ge(ident_zero, 1)
            nc.gpsimd.affine_select(out=ident[:, :], in_=ident[:, :], compare_op=ALU.not_equal, fill=1.0,
                                    base=0, pattern=[[-1, P]], channel_multiplier=1).then_inc(ident_ready, 1)

            def e_low(im, n):
                if low_on_vector(im, n):
                    return
                h, k = divmod(n, KC)
                pixels = slice(HALF * h, HALF * (h + 1))
                pool.wait_ge(e_ready, im.count(4, n))
                if not im.is_number(0):
                    pool.wait_ge(out_ready, im.at(-1).count(TILES, HT * h + HT - 1))
                nc.gpsimd.tensor_tensor(e_lo[:, k, pixels], e_sb[:, k, pixels], e_hi[:, k, pixels].bitcast(f32),
                                        ALU.subtract).then_inc(e_lo_ready, 1)

            def x_low(im, f):
                h, c = divmod(f, CC)
                pixels = slice(HALF * h, HALF * (h + 1))
                pool.wait_ge(xT_copied, im.count(4, f))
                if not im.is_number(0):
                    pool.wait_ge(g_ready, im.at(-1).count(2, h))
                nc.gpsimd.tensor_tensor(xT_lo[:, c, pixels], xT[:, c, pixels], xT_hi[:, c, pixels].bitcast(f32),
                                        ALU.subtract).then_inc(xT_lo_ready, 1)

            def G_low(im):
                pool.wait_ge(G_copied, im.count(1, 0))
                nc.gpsimd.tensor_tensor(G_lo[:, im.slot, :, 0:C], G_sb[:, :].rearrange("p (k c) -> p k c", k=KC),
                                        G_hi[:, im.slot, :, 0:C].bitcast(f32), ALU.subtract).then_inc(G_lo_ready, 1)

            def g_low(im):
                pool.wait_ge(g_hi_ready, im.count(1, 0))
                if not im.is_number(0):
                    pool.wait_ge(G_ready, im.at(-1).count(1, 0))
                nc.gpsimd.tensor_tensor(g_lo[:, :], g_max[:, :], g_hi[:, :].bitcast(f32),
                                        ALU.subtract).then_inc(g_lo_ready, 1)

            def step(im, front, back, turn):
                if back:
                    for n in range(4):
                        e_low(im.at(-1), n)
                if front:
                    g_low(im)
                if turn and not on_vector(im.at(1)):
                    for f in range(4):
                        x_low(im.at(1), f)
                if front:
                    G_low(im)

            run(pool, step)

        @block.vector
        def _(dve):
            v = nc.vector

            def x_low(im, f):
                h, c = divmod(f, CC)
                pixels = slice(HALF * h, HALF * (h + 1))
                dve.wait_ge(xT_copied, im.count(4, f))
                if not im.is_number(0):
                    dve.wait_ge(g_ready, im.at(-1).count(2, h))
                v.tensor_tensor(xT_lo[:, c, pixels], turn_banks[f % 2][:, :], xT_hi[:, c, pixels].bitcast(f32),
                                ALU.subtract).then_inc(xT_lo_ready, 1)

            def e_low(im, n):
                h, k = divmod(n, KC)
                pixels = slice(HALF * h, HALF * (h + 1))
                dve.wait_ge(e_ready, im.count(4, n))
                dve.wait_ge(out_ready, im.at(-1).count(TILES, HT * h + HT - 1))
                v.tensor_tensor(e_lo[:, k, pixels], e_sb[:, k, pixels], e_hi[:, k, pixels].bitcast(f32),
                                ALU.subtract).then_inc(e_lo_last, 1)

            def phi_pool(im, h):
                dve.wait_ge(tp_ready, im.count(2, h))
                if h == 0 and not im.is_number(0):
                    dve.wait_ge(phi_lo_ready, im.at(-1).count(1, 0))
                v.tensor_reduce(phi_max[2 * DK:THETA, P * h:P * (h + 1)],
                                proj_banks[h][THETA:P, :].rearrange("p (w n) -> p n w", w=WIN),
                                AX.X, ALU.max).then_inc(phi_pooled, 1)

            def theta_lo(im, h):
                rows, pixels = slice(DK, 2 * DK), slice(HALF * h, HALF * (h + 1))
                dve.wait_ge(theta_hi_ready, im.count(2, h))
                v.tensor_tensor(theta[rows, im.slot, pixels], proj_banks[h][rows, :],
                                theta[rows, im.slot, pixels].bitcast(f32), ALU.subtract).then_inc(theta_lo_ready, 1)

            def phi_parts(im):
                rows = slice(2 * DK, THETA)
                dve.wait_ge(phi_pooled, im.count(2, 1))
                v.tensor_copy(phi_hi[rows, :], phi_max[rows, :]).then_inc(phi_copied, 1)
                v.tensor_copy(phi[0:DK, im.slot, :], phi_max[rows, :])
                v.tensor_copy(phi[DK:2 * DK, im.slot, :], phi_max[rows, :])
                dve.wait_ge(phi_copied, im.count(1, 0))
                v.tensor_tensor(phi[rows, im.slot, :], phi_max[rows, :], phi_hi[rows, :].bitcast(f32),
                                ALU.subtract).then_inc(phi_lo_ready, 1)

            def g_pool(im, h):
                dve.wait_ge(g_ready, im.count(2, h))
                if h == 0 and not im.is_number(0):
                    dve.wait_ge(g_lo_ready, im.at(-1).count(1, 0))
                v.tensor_reduce(g_max[:, P * h:P * (h + 1)], proj_banks[h][:, :].rearrange("p (w n) -> p n w", w=WIN),
                                AX.X, ALU.max).then_inc(g_pooled, 1)

            def maxima(im, n):
                dve.wait_ge(score_ready, im.count(4, n))
                v.tensor_reduce(neg_max[:, 2 * n:2 * n + 2],
                                score_banks[n % 2][:, :].rearrange("p (t k) -> p t k", t=2),
                                AX.X, ALU.max, negate=True).then_inc(max_ready, 1)

            def max_hi(im):
                dve.wait_ge(max_ready, im.count(4, 3))
                if not im.is_number(0):
                    dve.wait_ge(neg_turned, im.at(-1).count(1, 0))
                v.tensor_copy(neg_parts[:, 0:TILES].bitcast(f32r), neg_max[:, :]).then_inc(neg_hi_ready, 1)

            def max_lo(im):
                dve.wait_ge(neg_hi_ready, im.count(1, 0))
                v.tensor_tensor(neg_parts[:, TILES:2 * TILES], neg_max[:, :], neg_parts[:, 0:TILES],
                                ALU.subtract).then_inc(neg_lo_ready, 1)

            def reciprocal(im, t):
                dve.wait_ge(out_ready, im.count(TILES, t))
                v.reciprocal(r_sum[:, t:t + 1], out_banks[t % 2][:, C:C + 1]).then_inc(r_ready, 1)

            def finish(im, t):
                dve.wait_ge(r_ready, im.count(TILES, t))
                if t % HT == 0 and not im.is_number(0):
                    dve.wait_ge(y_out[t // HT], im.number * 16)
                v.scalar_tensor_tensor(y_sb[:, t, :], out_banks[t % 2][:, 0:C], r_sum[:, t:t + 1],
                                       x_sb[:, im.slot, t, :], ALU.mult, ALU.add).then_inc(y_ready, 1)

            v.memset(neg_parts[:, :], 0.0).then_inc(fixed_ready, 1)
            v.memset(phi[THETA:STACK, :, :].bitcast(f32), 1.0).then_inc(fixed_ready, 1)
            v.memset(G_hi[:, :, :, C:GW].bitcast(f32), 1.0).then_inc(fixed_ready, 1)
            v.memset(G_lo[:, :, :, C:GW].bitcast(f32), 0.0).then_inc(fixed_ready, 1)

            def three(cols):
                return cols.rearrange("p a (n d) -> p a n d", d=DK)

            w_t3 = w_t_sb[:, :, :].unsqueeze(2).to_broadcast([P, CC, 3, DK])
            dve.wait_ge(w_tp_in, 2 * 16)
            v.tensor_copy(three(w_tp_hi[:, :, 0:THETA]), w_t3).then_inc(w_hi_ready, 1)
            v.tensor_copy(w_tp_hi[:, :, THETA:P], w_p_sb[:, :, :]).then_inc(w_hi_ready, 1)
            dve.wait_ge(w_hi_ready, 2)
            v.tensor_tensor(three(w_tp_lo[:, :, 0:THETA]), w_t3, three(w_tp_hi[:, :, 0:THETA].bitcast(f32)),
                            ALU.subtract).then_inc(w_lo_ready, 1)
            v.tensor_tensor(w_tp_lo[:, :, THETA:P], w_p_sb[:, :, :], w_tp_hi[:, :, THETA:P].bitcast(f32),
                            ALU.subtract).then_inc(w_lo_ready, 1)
            for f in range(2):
                x_low(Image(0, 0), f)
            dve.wait_ge(w_g_in, 16)
            v.tensor_copy(w_g_hi[:, :, :], w_g_sb[:, :, :]).then_inc(w_hi_ready, 1)
            for f in range(2, 4):
                x_low(Image(0, 0), f)
            dve.wait_ge(w_hi_ready, 3)
            v.tensor_tensor(w_g_lo[:, :, :], w_g_sb[:, :, :], w_g_hi[:, :, :].bitcast(f32),
                            ALU.subtract).then_inc(w_lo_ready, 1)

            def output_weights():
                dve.wait_ge(w_o_in, 2 * 16)
                v.tensor_scalar(w_og[:, :], w_o_sb[:, :], gamma_sb[:, 0:1], None, ALU.mult).then_inc(w_og_ready, 1)
                dve.wait_ge(w_og_ready, 1)
                v.tensor_copy(w_o_hi[:, :], w_og[:, :]).then_inc(w_hi_ready, 1)
                dve.wait_ge(w_hi_ready, 4)
                v.tensor_tensor(w_o_lo[:, :], w_og[:, :], w_o_hi[:, :].bitcast(f32),
                                ALU.subtract).then_inc(w_lo_ready, 1)

            def step(im, front, back, turn):
                old = im.at(-1)
                for n in range(4):
                    if low_on_vector(old, n):
                        e_low(old, n)
                if front:
                    for h in range(2):
                        phi_pool(im, h)
                        theta_lo(im, h)
                    phi_parts(im)
                    g_pool(im, 0)
                    g_pool(im, 1)
                if im.is_number(0):
                    output_weights()
                for t in range(TILES + 1):
                    if back and t > 0:
                        finish(old, t - 1)
                    if front and t < 4:
                        maxima(im, t)
                    if front and t == 3:
                        max_hi(im)
                    if back and t < TILES:
                        reciprocal(old, t)
                    if front and t == 3:
                        max_lo(im)
                    if turn and t < 4 and on_vector(im.at(1)):
                        x_low(im.at(1), t)

            run(dve, step)


_INS = ["x", "L0_conv_W_theta", "L0_conv_W_phi", "L0_conv_W_g", "L0_conv_W_o", "L0_conv_gamma"]


def kernel(**inputs):
    import numpy as _np
    import concourse.bacc as _bacc
    from concourse import mybir as _mybir
    from concourse.bass_utils import run_bass_kernel_spmd as _run

    nc = _bacc.Bacc("TRN2", target_bir_lowering=False, num_devices=1)
    arrays, args = {}, []
    for name in _INS:
        a = _np.atleast_1d(_np.ascontiguousarray(inputs[name]))
        arrays[f"in_{name}"] = a
        args.append(nc.dram_tensor(f"in_{name}", a.shape, _mybir.dt.from_np(a.dtype), kind="ExternalInput").ap())
    out = nc.dram_tensor("out", (B, H, W, C), _mybir.dt.float32, kind="ExternalOutput").ap()
    nonlocal_block(nc, *args, out)
    r = _run(nc, [arrays], core_ids=[0])
    return r.results[0]["out"]
```

```python
import concourse.bass as bass
from concourse import mybir
from contextlib import ExitStack

B, H, W, C = 16, 32, 32, 256
P = 128
DK = C // 8
DV = C // 2
Q = H * W
NK = Q // 4
WIN = 4
TILES = Q // P
CC = C // P
KC = NK // P
HALF = Q // 2
HT = TILES // 2
SLOTS = 3
TURNS = (B - 3) // SLOTS
THETA = 3 * DK
STACK = THETA + 2
GW = C + 2


class Image:

    def __init__(self, turn, k):
        self.turn, self.k = turn, k

    def at(self, more):
        return Image(self.turn, self.k + more)

    @property
    def number(self):
        return self.turn * SLOTS + self.k

    @property
    def slot(self):
        return self.k % SLOTS

    def is_number(self, n):
        return isinstance(self.turn, int) and self.number == n

    def count(self, per_image, n):
        return self.number * per_image + (n + 1)

    def dma_count(self):
        return (self.turn + (self.k // SLOTS + 1)) * 16


def nonlocal_block(nc, x, w_theta, w_phi, w_g, w_o, gamma, out):
    f32, f32r = mybir.dt.float32, mybir.dt.float32r
    ALU = mybir.AluOpType
    ACT = mybir.ActivationFunctionType
    AX = mybir.AxisListType

    def by_cell(t):
        return t.rearrange("b (j yp dy) (xp dx) c -> b j xp yp dy (dx c)", j=2, dy=2, dx=2)

    x_cells, out_cells = by_cell(x), by_cell(out)

    ctx = ExitStack()
    with ctx:
        def sb(name, shape, dt=f32):
            return ctx.enter_context(nc.sbuf_tensor(name, shape, dt))

        def bank(name):
            return ctx.enter_context(nc.psum_tensor(name, [P, HALF], f32))

        def sem(name):
            return ctx.enter_context(nc.semaphore(name))

        ident = sb("ident", [P, P])
        w_t_sb, w_p_sb = sb("w_t_sb", [P, CC, DK]), sb("w_p_sb", [P, CC, DK])
        w_tp_hi, w_tp_lo = sb("w_tp_hi", [P, CC, P], f32r), sb("w_tp_lo", [P, CC, P], f32r)
        w_g_sb = sb("w_g_sb", [P, CC, DV])
        w_g_hi, w_g_lo = sb("w_g_hi", [P, CC, DV], f32r), sb("w_g_lo", [P, CC, DV], f32r)
        w_o_sb, w_og = sb("w_o_sb", [P, C]), sb("w_og", [P, C])
        w_o_hi, w_o_lo = sb("w_o_hi", [P, C], f32r), sb("w_o_lo", [P, C], f32r)
        gamma_sb = sb("gamma_sb", [P, 1])
        x_sb = sb("x_sb", [P, SLOTS, TILES, C])
        y_sb = sb("y_sb", [P, TILES, C])
        xT = sb("xT", [P, CC, Q])
        xT_hi, xT_lo = sb("xT_hi", [P, SLOTS, CC, Q], f32r), sb("xT_lo", [P, SLOTS, CC, Q], f32r)
        theta = sb("theta", [P, SLOTS, Q], f32r)
        phi = sb("phi", [P, SLOTS, NK], f32r)
        phi_max = sb("phi_max", [P, NK])
        phi_hi = sb("phi_hi", [P, NK], f32r)
        g_max = sb("g_max", [P, NK])
        g_hi, g_lo = sb("g_hi", [P, NK], f32r), sb("g_lo", [P, NK], f32r)
        G_sb = sb("G_sb", [P, KC * C])
        G_hi, G_lo = sb("G_hi", [P, SLOTS, KC, GW], f32r), sb("G_lo", [P, SLOTS, KC, GW], f32r)
        neg_max = sb("neg_max", [P, TILES])
        neg_parts = sb("neg_parts", [P, P])
        neg_rows = sb("neg_rows", [2 * TILES, P], f32r)
        e_sb = sb("e_sb", [P, KC, Q])
        e_hi, e_lo = sb("e_hi", [P, KC, Q], f32r), sb("e_lo", [P, KC, Q], f32r)
        r_sum = sb("r_sum", [P, TILES])

        turn_banks = [bank("turn0"), bank("turn1")]
        proj_banks = [bank("proj0"), bank("proj1")]
        score_banks = [bank("score0"), bank("score1")]
        out_banks = [bank("out0"), bank("out1")]
        neg_bank, G_bank = score_banks

        def turn_bank(im, f):
            return ((turn_banks + out_banks)[f] if im.is_number(0) or im.is_number(1) else turn_banks[f % 2])

        def edge(im):
            return im.is_number(0) or im.is_number(B - 1)

        def score_bank(im, n):
            if edge(im):
                return (score_banks + turn_banks)[n]
            return turn_banks[1] if im.is_number(1) and n == 1 else score_banks[n % 2]

        def shifted_bank(im, n):
            return ([score_banks[0]] + turn_banks + [score_banks[1]] if edge(im) else score_banks + turn_banks)[n]

        def more_out_banks(im):
            return im.is_number(B - 2) or im.is_number(B - 1)

        def out_bank(im, t):
            return ((out_banks + proj_banks)[t % 4] if more_out_banks(im) else out_banks[t % 2])

        w_tp_in, w_g_in, w_o_in = sem("w_tp_in"), sem("w_g_in"), sem("w_o_in")
        w_hi_ready, w_lo_ready = sem("w_hi_ready"), sem("w_lo_ready")
        fixed_ready = sem("fixed_ready")
        w_og_ready = sem("w_og_ready")
        ident_zero, ident_ready = sem("ident_zero"), sem("ident_ready")
        x_in = [[sem(f"x_in{s}{h}") for h in range(2)] for s in range(SLOTS)]
        y_out = [sem(f"y_out{h}") for h in range(2)]
        last_out = [sem(f"last_out{dy}") for dy in range(2)]
        xT_turned = sem("xT_turned")
        xT_copied, xT_lo_ready = sem("xT_copied"), sem("xT_lo_ready")
        tp_ready, g_ready = sem("tp_ready"), sem("g_ready")
        theta_hi_ready, theta_lo_ready = sem("theta_hi_ready"), sem("theta_lo_ready")
        phi_pooled = sem("phi_pooled")
        phi_copied = sem("phi_copied")
        phi_lo_ready = sem("phi_lo_ready")
        g_pooled = sem("g_pooled")
        g_hi_ready, g_lo_ready = sem("g_hi_ready"), sem("g_lo_ready")
        G_ready = sem("G_ready")
        G_copied, G_lo_ready = sem("G_copied"), sem("G_lo_ready")
        score_ready = sem("score_ready")
        max_ready = sem("max_ready")
        neg_hi_ready, neg_lo_ready = sem("neg_hi_ready"), sem("neg_lo_ready")
        neg_turned = sem("neg_turned")
        neg_rows_ready = sem("neg_rows_ready")
        neg_in = [sem(f"neg_in{s}") for s in range(SLOTS)]
        shifted_ready = sem("shifted_ready")
        e_ready, e_lo_ready = sem("e_ready"), sem("e_lo_ready")
        e_lo_on_vector = sem("e_lo_on_vector")
        out_ready = sem("out_ready")
        r_ready = sem("r_ready")
        y_ready = sem("y_ready")

        block = ctx.enter_context(nc.Block())

        def on_vector(im):
            return im.is_number(0)

        def first_in_slot(im):
            return any(im.is_number(n) for n in range(SLOTS))

        def low_on_vector(im, n):
            return (im.is_number(0) and n == 1) or (im.is_number(B - 1) and n % 2 == 1)

        def vector_count(im, n):
            return 1 if im.is_number(0) else 2 + n // 2

        def run(eng, step, begin=None, end=None):
            if begin:
                begin(Image(0, 0))
            else:
                step(Image(0, 0), front=True, back=False, turn=True)
                step(Image(0, 1), front=True, back=True, turn=True)
            with eng.Fori(0, TURNS) as turn:
                for k in range(2, 2 + SLOTS):
                    step(Image(turn, k), front=True, back=True, turn=True)
            for k in range(2 + TURNS * SLOTS, B - 1):
                step(Image(0, k), front=True, back=True, turn=True)
            if end:
                end(Image(0, B - 1))
            else:
                step(Image(0, B - 1), front=True, back=True, turn=False)
                step(Image(0, B), front=False, back=True, turn=False)

        @block.sync
        def _(sp):
            def load(im, h):
                sp.dma_start(x_sb[:, im.slot, HT * h:HT * (h + 1), :].rearrange("p (dy dx) c -> p dy (dx c)", dy=2),
                             x_cells[im.number, h]).then_inc(x_in[im.slot][h], 16)

            def store(im, h):
                sp.wait_ge(y_ready, im.count(TILES, HT * h + HT - 1))
                sp.dma_start(out_cells[im.number, h],
                             y_sb[:, HT * h:HT * (h + 1), :].rearrange("p (dy dx) c -> p dy (dx c)", dy=2),
                             ).then_inc(y_out[h], 16)

            def store_row(im, h, dy):
                t = HT * h + 2 * dy
                sp.wait_ge(y_ready, im.count(TILES, t + 1))
                sp.dma_start(out_cells[im.number, h, :, :, dy],
                             y_sb[:, t:t + 2, :].rearrange("p dx c -> p (dx c)")).then_inc(last_out[dy], 16)

            load(Image(0, 0), 0)
            sp.dma_start(w_t_sb[:, :, :], w_theta.rearrange("(a p) n -> p a n", p=P)).then_inc(w_tp_in, 16)
            sp.dma_start(w_p_sb[:, :, :], w_phi.rearrange("(a p) n -> p a n", p=P)).then_inc(w_tp_in, 16)
            sp.dma_start(w_g_sb[:, :, :], w_g.rearrange("(a p) n -> p a n", p=P)).then_inc(w_g_in, 16)
            load(Image(0, 0), 1)
            sp.dma_start(w_o_sb[:, :], w_o).then_inc(w_o_in, 16)
            sp.dma_start(gamma_sb[:, :], gamma.partition_broadcast(P)).then_inc(w_o_in, 16)
            for n in range(1, SLOTS):
                load(Image(0, n), 0)
                load(Image(0, n), 1)

            def max_into_stack(im):
                sp.wait_ge(neg_rows_ready, im.count(1, 0))
                sp.dma_start(theta[THETA:STACK, im.slot, :].bitcast(f32).rearrange("r (t n) -> r t n", t=TILES),
                             neg_rows[:, :].bitcast(f32)).then_inc(neg_in[im.slot], 16)

            def step(im, front, back, turn):
                if front:
                    max_into_stack(im)
                if back:
                    for h in range(2):
                        if im.is_number(B) and h == 1:
                            store_row(im.at(-1), h, 0)
                            store_row(im.at(-1), h, 1)
                        else:
                            store(im.at(-1), h)
                        if not any(im.at(SLOTS - 1).is_number(n) for n in (B, B + 1, B + 2)):
                            load(im.at(SLOTS - 1), h)

            run(sp, step)
            sp.wait_ge(y_out[0], 16 * B)
            sp.wait_ge(y_out[1], 16 * (B - 1))
            for dy in range(2):
                sp.wait_ge(last_out[dy], 16)

        @block.tensor
        def _(pe):
            def turn_x(im, f):
                h, c = divmod(f, CC)
                pe.wait_ge(x_in[im.slot][h], im.dma_count())
                if im.is_number(1):
                    pe.wait_ge(xT_lo_ready, im.at(-1).count(4, f))
                elif im.is_number(2) and f < 2:
                    if f == 0:
                        pe.wait_ge(e_ready, im.at(-2).count(4, 1))
                    else:
                        pe.wait_ge(max_ready, im.at(-1).count(4, 1))
                elif f >= 2 and not im.is_number(0):
                    pe.wait_ge(xT_copied, im.count(4, f - 2))
                elif not im.is_number(0):
                    pe.wait_ge(e_ready, im.at(-2).count(4, f + 2))
                for t in range(HT):
                    last = nc.tensor.transpose(turn_bank(im, f)[:, P * t:P * (t + 1)],
                                               x_sb[:, im.slot, HT * h + t, P * c:P * (c + 1)], ident[:, :])
                last.then_inc(xT_turned, 1)

            def project(im, hi, lo, h, bank, done):
                for c in range(CC):
                    for n, (w, xT) in enumerate(((hi, xT_hi), (lo, xT_hi), (hi, xT_lo))):
                        last = nc.tensor.matmul(bank[:, :], w[:, c, :], xT[:, im.slot, c, HALF * h:HALF * (h + 1)],
                                                start=(c == 0 and n == 0), stop=(c == CC - 1 and n == 2))
                last.then_inc(done, 1)

            def theta_phi(im, h):
                if im.is_number(0):
                    pe.wait_ge(w_lo_ready, 2)
                    pe.wait_ge(fixed_ready, 4)
                pe.wait_ge(xT_lo_ready, im.count(4, CC * h + CC - 1))
                if not im.is_number(0):
                    pe.wait_ge(g_pooled, im.at(-1).count(2, h))
                project(im, w_tp_hi, w_tp_lo, h, proj_banks[h], tp_ready)

            def values(im, h):
                if im.is_number(0):
                    pe.wait_ge(w_lo_ready, 3)
                pe.wait_ge(theta_lo_ready, im.count(2, h))
                project(im, w_g_hi, w_g_lo, h, proj_banks[h], g_ready)

            def score(im, n):
                if n == 0:
                    pe.wait_ge(theta_lo_ready, im.count(2, 1))
                    pe.wait_ge(phi_lo_ready, im.count(1, 0))
                if im.is_number(0):
                    if n >= 2:
                        pe.wait_ge(xT_copied, im.at(1).count(4, n - 2))
                elif im.is_number(B - 1):
                    pe.wait_ge(e_ready, im.at(-1).count(4, n))
                elif im.is_number(1) and n != 2:
                    pe.wait_ge(e_ready, im.at(-1).count(4, 2 if n == 1 else n))
                elif n >= 2:
                    pe.wait_ge(max_ready, im.count(4, n - 2))
                else:
                    pe.wait_ge(e_ready, im.at(-1).count(4, n))
                for i in range(2):
                    t = 2 * n + i
                    last = nc.tensor.matmul(score_bank(im, n)[:, NK * i:NK * (i + 1)],
                                            theta[0:THETA, im.slot, P * t:P * (t + 1)],
                                            phi[0:THETA, im.slot, :], start=(i == 0), stop=True,
                                            skip_group_check=True)
                last.then_inc(score_ready, 1)

            def turn_max(im):
                pe.wait_ge(neg_lo_ready, im.count(1, 0))
                pe.wait_ge(max_ready, im.count(4, 2))
                nc.tensor.transpose(neg_bank[:, 0:P], neg_parts[:, :], ident[:, :]).then_inc(neg_turned, 1)

            def shifted(im, n):
                h, k = divmod(n, KC)
                if n == 0:
                    pe.wait_ge(neg_rows_ready, im.count(1, 0))
                    pe.wait_ge(neg_in[im.slot], im.dma_count())
                elif n == (3 if edge(im) else 1):
                    pe.wait_ge(G_copied, im.count(1, 0))
                elif not edge(im):
                    pe.wait_ge(xT_copied, im.at(1).count(4, n))
                nc.tensor.matmul(shifted_bank(im, n)[:, :], phi[0:STACK, im.slot, P * k:P * (k + 1)],
                                 theta[0:STACK, im.slot, HALF * h:HALF * (h + 1)],
                                 start=True, stop=True).then_inc(shifted_ready, 1)

            def mix(im):
                if im.is_number(0):
                    pe.wait_ge(w_lo_ready, 4)
                pe.wait_ge(g_hi_ready, im.count(1, 0))
                pe.wait_ge(g_lo_ready, im.count(1, 0))
                pe.wait_ge(max_ready, im.count(4, 3))
                n = 0
                for k in range(KC):
                    cells = slice(P * k, P * (k + 1))
                    for g, w in ((g_hi, w_o_hi), (g_hi, w_o_lo), (g_lo, w_o_hi)):
                        last = nc.tensor.matmul(G_bank[:, C * k:C * (k + 1)], g[:, cells], w[:, :],
                                                start=(n == 0), stop=(n % 3 == 2), skip_group_check=True)
                        n += 1
                last.then_inc(G_ready, 1)

            def output(im, t):
                if t == 0:
                    pe.wait_ge(G_lo_ready, im.count(1, 0))
                if t % HT == 0:
                    n = KC * (t // HT) + KC - 1
                    pe.wait_ge(e_lo_ready, im.count(4, n))
                    if low_on_vector(im, n):
                        pe.wait_ge(e_lo_on_vector, vector_count(im, n))
                if im.is_number(B - 2) and 2 <= t < 4:
                    pe.wait_ge(g_pooled, im.at(1).count(2, t - 2))
                elif im.is_number(B - 1) or (im.is_number(B - 2) and t >= 4):
                    pe.wait_ge(y_ready, im.count(TILES, t - 4))
                elif im.is_number(0) and t < 2:
                    pe.wait_ge(xT_copied, im.at(1).count(4, t + 2))
                else:
                    pe.wait_ge(y_ready, im.count(TILES, t - 2))
                n = 0
                for k in range(KC):
                    pixels = slice(P * t, P * (t + 1))
                    for e, G in ((e_hi, G_hi), (e_hi, G_lo), (e_lo, G_hi)):
                        last = nc.tensor.matmul(out_bank(im, t)[:, 0:GW], e[:, k, pixels], G[:, im.slot, k, :],
                                                start=(n == 0), stop=(n == 3 * KC - 1))
                        n += 1
                last.then_inc(out_ready, 1)

            def projections(im, old):
                theta_phi(im, 0)
                shifted(old, 0)
                shifted(old, 1)
                theta_phi(im, 1)
                shifted(old, 2)
                values(im, 0)
                shifted(old, 3)
                values(im, 1)

            def step(im, front, back, turn):
                old = im.at(-1)
                projections(im, old)
                score(im, 0)
                score(im, 1)
                for t in range(TILES):
                    if t == 5:
                        turn_max(im)
                    if t == 6:
                        mix(im)
                    output(old, t)
                    if t in (1, 2):
                        score(im, t + 1)
                    if t < 4:
                        turn_x(im.at(1), t)

            def begin(im):
                new, newer = im.at(1), im.at(2)
                pe.wait_ge(ident_ready, 1)
                for f in range(4):
                    turn_x(im, f)
                theta_phi(im, 0)
                theta_phi(im, 1)
                turn_x(new, 0)
                turn_x(new, 1)
                values(im, 0)
                turn_x(new, 2)
                for n in range(4):
                    score(im, n)
                turn_x(new, 3)
                values(im, 1)
                theta_phi(new, 0)
                turn_max(im)
                theta_phi(new, 1)
                mix(im)
                values(new, 0)
                for n in range(4):
                    shifted(im, n)
                values(new, 1)
                score(new, 0)
                turn_x(newer, 0)
                score(new, 1)
                for t in range(TILES):
                    if t == 5:
                        turn_max(new)
                    if t == 6:
                        mix(new)
                    output(im, t)
                    if t in (1, 2):
                        score(new, t + 1)
                    if t in (1, 2, 3):
                        turn_x(newer, t)

            def end(im):
                old = im.at(-1)
                projections(im, old)
                for n in range(4):
                    score(im, n)
                for t in range(TILES):
                    if t == 3:
                        turn_max(im)
                    if t == 5:
                        mix(im)
                    output(old, t)
                    if t == 5:
                        shifted(im, 0)
                        shifted(im, 1)
                    if t == 6:
                        shifted(im, 2)
                shifted(im, 3)
                for t in range(TILES):
                    output(im, t)

            run(pe, step, begin, end)

        @block.scalar
        def _(act):
            def x_copies(im, f):
                h, c = divmod(f, CC)
                act.wait_ge(xT_turned, im.count(4, f))
                if not first_in_slot(im):
                    act.wait_ge(g_ready, im.at(-SLOTS).count(2, h))
                if not im.is_number(0):
                    act.wait_ge(xT_lo_ready, im.at(-1).count(4, f))
                high = nc.scalar.copy(xT_hi[:, im.slot, c, HALF * h:HALF * (h + 1)], turn_bank(im, f)[:, :])
                if on_vector(im):
                    high.then_inc(xT_copied, 1)
                    return
                nc.scalar.copy(xT[:, c, HALF * h:HALF * (h + 1)], turn_bank(im, f)[:, :]).then_inc(xT_copied, 1)

            def theta_hi(im, h):
                act.wait_ge(tp_ready, im.count(2, h))
                nc.scalar.copy(theta[0:THETA, im.slot, HALF * h:HALF * (h + 1)],
                               proj_banks[h][0:THETA, :]).then_inc(theta_hi_ready, 1)

            def exp_high(im, n):
                h, k = divmod(n, KC)
                pixels = slice(HALF * h, HALF * (h + 1))
                act.wait_ge(shifted_ready, im.count(4, n))
                if not im.is_number(0):
                    act.wait_ge(out_ready, im.at(-1).count(TILES, HT * h + HT - 1))
                nc.scalar.activation(e_hi[:, k, pixels], shifted_bank(im, n)[:, :], ACT.Exp)

            def exp_whole(im, n):
                h, k = divmod(n, KC)
                pixels = slice(HALF * h, HALF * (h + 1))
                if not im.is_number(0):
                    act.wait_ge(e_lo_ready, im.at(-1).count(4, n))
                if low_on_vector(im.at(-1), n):
                    act.wait_ge(e_lo_on_vector, vector_count(im.at(-1), n))
                nc.scalar.activation(e_sb[:, k, pixels], shifted_bank(im, n)[:, :], ACT.Exp).then_inc(e_ready, 1)

            def G_copies(im):
                act.wait_ge(G_ready, im.count(1, 0))
                if not im.is_number(0):
                    act.wait_ge(G_lo_ready, im.at(-1).count(1, 0))
                nc.scalar.copy(G_hi[:, im.slot, :, 0:C], G_bank[:, :].rearrange("p (k c) -> p k c", k=KC))
                nc.scalar.copy(G_sb[:, :], G_bank[:, :]).then_inc(G_copied, 1)

            def g_high(im):
                act.wait_ge(g_pooled, im.count(2, 1))
                if not im.is_number(0):
                    act.wait_ge(G_ready, im.at(-1).count(1, 0))
                nc.scalar.copy(g_hi[:, :], g_max[:, :]).then_inc(g_hi_ready, 1)

            def max_rows(im):
                act.wait_ge(neg_turned, im.count(1, 0))
                if not im.is_number(0):
                    act.wait_ge(neg_in[(im.k - 1) % SLOTS], im.at(-1).dma_count())
                nc.scalar.copy(neg_rows[:, :], neg_bank[0:2 * TILES, 0:P]).then_inc(neg_rows_ready, 1)

            def step(im, front, back, turn):
                old = im.at(-1)
                if front:
                    theta_hi(im, 0)
                if back:
                    exp_high(old, 0)
                    exp_whole(old, 0)
                if front:
                    theta_hi(im, 1)
                if back:
                    for n in range(1, 4):
                        exp_high(old, n)
                        exp_whole(old, n)
                if front:
                    g_high(im)
                if turn:
                    for f in range(4):
                        x_copies(im.at(1), f)
                if front:
                    max_rows(im)
                    G_copies(im)

            def begin(im):
                new, newer = im.at(1), im.at(2)
                for f in range(4):
                    x_copies(im, f)
                theta_hi(im, 0)
                theta_hi(im, 1)
                for f in range(4):
                    x_copies(new, f)
                g_high(im)
                theta_hi(new, 0)
                max_rows(im)
                theta_hi(new, 1)
                G_copies(im)
                for n in range(4):
                    exp_high(im, n)
                    exp_whole(im, n)
                x_copies(newer, 0)
                g_high(new)
                for f in range(1, 4):
                    x_copies(newer, f)
                max_rows(new)
                G_copies(new)

            run(act, step, begin)

        @block.gpsimd
        def _(pool):
            nc.gpsimd.memset(ident[:, :], 0.0).then_inc(ident_zero, 1)
            pool.wait_ge(ident_zero, 1)
            nc.gpsimd.affine_select(out=ident[:, :], in_=ident[:, :], compare_op=ALU.not_equal, fill=1.0,
                                    base=0, pattern=[[-1, P]], channel_multiplier=1).then_inc(ident_ready, 1)

            def e_low(im, n):
                if low_on_vector(im, n):
                    return
                h, k = divmod(n, KC)
                pixels = slice(HALF * h, HALF * (h + 1))
                pool.wait_ge(e_ready, im.count(4, n))
                if not im.is_number(0):
                    pool.wait_ge(out_ready, im.at(-1).count(TILES, HT * h + HT - 1))
                nc.gpsimd.tensor_tensor(e_lo[:, k, pixels], e_sb[:, k, pixels], e_hi[:, k, pixels].bitcast(f32),
                                        ALU.subtract).then_inc(e_lo_ready, 2 if low_on_vector(im, n + 1) else 1)

            def x_low(im, f):
                h, c = divmod(f, CC)
                pixels = slice(HALF * h, HALF * (h + 1))
                pool.wait_ge(xT_copied, im.count(4, f))
                if not first_in_slot(im):
                    pool.wait_ge(g_ready, im.at(-SLOTS).count(2, h))
                nc.gpsimd.tensor_tensor(xT_lo[:, im.slot, c, pixels], xT[:, c, pixels],
                                        xT_hi[:, im.slot, c, pixels].bitcast(f32), ALU.subtract).then_inc(xT_lo_ready, 1)

            def G_low(im):
                if edge(im):
                    return
                pool.wait_ge(G_copied, im.count(1, 0))
                nc.gpsimd.tensor_tensor(G_lo[:, im.slot, :, 0:C], G_sb[:, :].rearrange("p (k c) -> p k c", k=KC),
                                        G_hi[:, im.slot, :, 0:C].bitcast(f32), ALU.subtract).then_inc(G_lo_ready, 1)

            def g_low(im):
                pool.wait_ge(g_hi_ready, im.count(1, 0))
                if not im.is_number(0):
                    pool.wait_ge(G_ready, im.at(-1).count(1, 0))
                nc.gpsimd.tensor_tensor(g_lo[:, :], g_max[:, :], g_hi[:, :].bitcast(f32),
                                        ALU.subtract).then_inc(g_lo_ready, 1)

            def step(im, front, back, turn):
                if back:
                    for n in range(4):
                        e_low(im.at(-1), n)
                if front:
                    g_low(im)
                if turn:
                    for f in range(4):
                        x_low(im.at(1), f)
                if front:
                    G_low(im)

            def begin(im):
                new, newer = im.at(1), im.at(2)
                for f in range(4):
                    x_low(new, f)
                g_low(im)
                for n in range(4):
                    e_low(im, n)
                g_low(new)
                for f in range(4):
                    x_low(newer, f)
                G_low(new)

            run(pool, step, begin)

        @block.vector
        def _(dve):
            v = nc.vector

            def x_low(im, f):
                h, c = divmod(f, CC)
                pixels = slice(HALF * h, HALF * (h + 1))
                dve.wait_ge(xT_copied, im.count(4, f))
                v.tensor_tensor(xT_lo[:, im.slot, c, pixels], turn_bank(im, f)[:, :],
                                xT_hi[:, im.slot, c, pixels].bitcast(f32), ALU.subtract).then_inc(xT_lo_ready, 1)

            def e_low(im, n):
                h, k = divmod(n, KC)
                pixels = slice(HALF * h, HALF * (h + 1))
                dve.wait_ge(e_ready, im.count(4, n))
                if not im.is_number(0):
                    dve.wait_ge(out_ready, im.at(-1).count(TILES, HT * h + HT - 1))
                v.tensor_tensor(e_lo[:, k, pixels], e_sb[:, k, pixels], e_hi[:, k, pixels].bitcast(f32),
                                ALU.subtract).then_inc(e_lo_on_vector, 1)

            def G_low(im):
                dve.wait_ge(G_copied, im.count(1, 0))
                v.tensor_tensor(G_lo[:, im.slot, :, 0:C], G_sb[:, :].rearrange("p (k c) -> p k c", k=KC),
                                G_hi[:, im.slot, :, 0:C].bitcast(f32), ALU.subtract).then_inc(G_lo_ready, 1)

            def phi_pool(im, h):
                dve.wait_ge(tp_ready, im.count(2, h))
                if h == 0 and not im.is_number(0):
                    dve.wait_ge(phi_lo_ready, im.at(-1).count(1, 0))
                v.tensor_reduce(phi_max[2 * DK:THETA, P * h:P * (h + 1)],
                                proj_banks[h][THETA:P, :].rearrange("p (w n) -> p n w", w=WIN),
                                AX.X, ALU.max).then_inc(phi_pooled, 1)

            def theta_lo(im, h):
                rows, pixels = slice(DK, 2 * DK), slice(HALF * h, HALF * (h + 1))
                dve.wait_ge(theta_hi_ready, im.count(2, h))
                v.tensor_tensor(theta[rows, im.slot, pixels], proj_banks[h][rows, :],
                                theta[rows, im.slot, pixels].bitcast(f32), ALU.subtract).then_inc(theta_lo_ready, 1)

            def phi_parts(im):
                rows = slice(2 * DK, THETA)
                dve.wait_ge(phi_pooled, im.count(2, 1))
                v.tensor_copy(phi_hi[rows, :], phi_max[rows, :]).then_inc(phi_copied, 1)
                v.tensor_copy(phi[0:DK, im.slot, :], phi_max[rows, :])
                v.tensor_copy(phi[DK:2 * DK, im.slot, :], phi_max[rows, :])
                dve.wait_ge(phi_copied, im.count(1, 0))
                v.tensor_tensor(phi[rows, im.slot, :], phi_max[rows, :], phi_hi[rows, :].bitcast(f32),
                                ALU.subtract).then_inc(phi_lo_ready, 1)

            def g_pool(im, h):
                dve.wait_ge(g_ready, im.count(2, h))
                if h == 0 and not im.is_number(0):
                    dve.wait_ge(g_lo_ready, im.at(-1).count(1, 0))
                v.tensor_reduce(g_max[:, P * h:P * (h + 1)], proj_banks[h][:, :].rearrange("p (w n) -> p n w", w=WIN),
                                AX.X, ALU.max).then_inc(g_pooled, 1)

            def maxima(im, n):
                dve.wait_ge(score_ready, im.count(4, n))
                v.tensor_reduce(neg_max[:, 2 * n:2 * n + 2],
                                score_bank(im, n)[:, :].rearrange("p (t k) -> p t k", t=2),
                                AX.X, ALU.max, negate=True).then_inc(max_ready, 1)

            def max_hi(im):
                dve.wait_ge(max_ready, im.count(4, 3))
                if not im.is_number(0):
                    dve.wait_ge(neg_turned, im.at(-1).count(1, 0))
                v.tensor_copy(neg_parts[:, 0:TILES].bitcast(f32r), neg_max[:, :]).then_inc(neg_hi_ready, 1)

            def max_lo(im):
                dve.wait_ge(neg_hi_ready, im.count(1, 0))
                v.tensor_tensor(neg_parts[:, TILES:2 * TILES], neg_max[:, :], neg_parts[:, 0:TILES],
                                ALU.subtract).then_inc(neg_lo_ready, 1)

            def reciprocal(im, t):
                dve.wait_ge(out_ready, im.count(TILES, t))
                v.reciprocal(r_sum[:, t:t + 1], out_bank(im, t)[:, C:C + 1]).then_inc(r_ready, 1)

            def finish(im, t):
                dve.wait_ge(r_ready, im.count(TILES, t))
                if t % HT == 0 and not im.is_number(0):
                    dve.wait_ge(y_out[t // HT], im.number * 16)
                v.scalar_tensor_tensor(y_sb[:, t, :], out_bank(im, t)[:, 0:C], r_sum[:, t:t + 1],
                                       x_sb[:, im.slot, t, :], ALU.mult, ALU.add).then_inc(y_ready, 1)

            v.memset(neg_parts[:, :], 0.0).then_inc(fixed_ready, 1)
            v.memset(phi[THETA:STACK, :, :].bitcast(f32), 1.0).then_inc(fixed_ready, 1)
            v.memset(G_hi[:, :, :, C:GW].bitcast(f32), 1.0).then_inc(fixed_ready, 1)
            v.memset(G_lo[:, :, :, C:GW].bitcast(f32), 0.0).then_inc(fixed_ready, 1)

            def three(cols):
                return cols.rearrange("p a (n d) -> p a n d", d=DK)

            w_t3 = w_t_sb[:, :, :].unsqueeze(2).to_broadcast([P, CC, 3, DK])
            dve.wait_ge(w_tp_in, 2 * 16)
            v.tensor_copy(three(w_tp_hi[:, :, 0:THETA]), w_t3).then_inc(w_hi_ready, 1)
            v.tensor_copy(w_tp_hi[:, :, THETA:P], w_p_sb[:, :, :]).then_inc(w_hi_ready, 1)
            dve.wait_ge(w_hi_ready, 2)
            v.tensor_tensor(three(w_tp_lo[:, :, 0:THETA]), w_t3, three(w_tp_hi[:, :, 0:THETA].bitcast(f32)),
                            ALU.subtract).then_inc(w_lo_ready, 1)
            v.tensor_tensor(w_tp_lo[:, :, THETA:P], w_p_sb[:, :, :], w_tp_hi[:, :, THETA:P].bitcast(f32),
                            ALU.subtract).then_inc(w_lo_ready, 1)
            for f in range(2):
                x_low(Image(0, 0), f)
            dve.wait_ge(w_g_in, 16)
            v.tensor_copy(w_g_hi[:, :, :], w_g_sb[:, :, :]).then_inc(w_hi_ready, 1)
            for f in range(2, 4):
                x_low(Image(0, 0), f)
            dve.wait_ge(w_hi_ready, 3)
            v.tensor_tensor(w_g_lo[:, :, :], w_g_sb[:, :, :], w_g_hi[:, :, :].bitcast(f32),
                            ALU.subtract).then_inc(w_lo_ready, 1)
            dve.wait_ge(w_o_in, 2 * 16)
            v.tensor_scalar(w_og[:, :], w_o_sb[:, :], gamma_sb[:, 0:1], None, ALU.mult).then_inc(w_og_ready, 1)
            dve.wait_ge(w_og_ready, 1)
            v.tensor_copy(w_o_hi[:, :], w_og[:, :]).then_inc(w_hi_ready, 1)
            dve.wait_ge(w_hi_ready, 4)
            v.tensor_tensor(w_o_lo[:, :], w_og[:, :], w_o_hi[:, :].bitcast(f32),
                            ALU.subtract).then_inc(w_lo_ready, 1)

            def maxima_and_output(im, old):
                maxima(im, 0)
                for t in range(TILES):
                    reciprocal(old, t)
                    if t < 3:
                        maxima(im, t + 1)
                    if t == 3:
                        max_hi(im)
                    finish(old, t)
                    if t == 3:
                        max_lo(im)

            def step(im, front, back, turn):
                for h in range(2):
                    phi_pool(im, h)
                    theta_lo(im, h)
                phi_parts(im)
                g_pool(im, 0)
                g_pool(im, 1)
                maxima_and_output(im, im.at(-1))

            def begin(im):
                new = im.at(1)
                for h in range(2):
                    phi_pool(im, h)
                    theta_lo(im, h)
                phi_parts(im)
                g_pool(im, 0)
                maxima(im, 0)
                maxima(im, 1)
                maxima(im, 2)
                maxima(im, 3)
                max_hi(im)
                g_pool(im, 1)
                max_lo(im)
                for h in range(2):
                    phi_pool(new, h)
                    theta_lo(new, h)
                phi_parts(new)
                G_low(im)
                g_pool(new, 0)
                e_low(im, 1)
                g_pool(new, 1)
                maxima_and_output(new, im)

            def end(im):
                old = im.at(-1)
                for h in range(2):
                    phi_pool(im, h)
                    theta_lo(im, h)
                phi_parts(im)
                g_pool(im, 0)
                for n in range(4):
                    maxima(im, n)
                max_hi(im)
                reciprocal(old, 0)
                max_lo(im)
                g_pool(im, 1)
                for t in range(1, TILES):
                    finish(old, t - 1)
                    if t == TILES - 2:
                        G_low(im)
                    if t == TILES - 1:
                        e_low(im, 1)
                    reciprocal(old, t)
                finish(old, TILES - 1)
                reciprocal(im, 0)
                e_low(im, 3)
                for t in range(1, TILES):
                    finish(im, t - 1)
                    reciprocal(im, t)
                finish(im, TILES - 1)

            run(dve, step, begin, end)


_INS = ["x", "L0_conv_W_theta", "L0_conv_W_phi", "L0_conv_W_g", "L0_conv_W_o", "L0_conv_gamma"]


def kernel(**inputs):
    import numpy as _np
    import concourse.bacc as _bacc
    from concourse import mybir as _mybir
    from concourse.bass_utils import run_bass_kernel_spmd as _run

    nc = _bacc.Bacc("TRN2", target_bir_lowering=False, num_devices=1)
    arrays, args = {}, []
    for name in _INS:
        a = _np.atleast_1d(_np.ascontiguousarray(inputs[name]))
        arrays[f"in_{name}"] = a
        args.append(nc.dram_tensor(f"in_{name}", a.shape, _mybir.dt.from_np(a.dtype), kind="ExternalInput").ap())
    out = nc.dram_tensor("out", (B, H, W, C), _mybir.dt.float32, kind="ExternalOutput").ap()
    nonlocal_block(nc, *args, out)
    r = _run(nc, [arrays], core_ids=[0])
    return r.results[0]["out"]
```
